# Optimizing a Trainium2 kernel written in Bass

```python
import numpy as np
import jax
import jax.numpy as jnp

def _softmax(x, axis=-1):
    return jax.nn.softmax(x, axis=axis)

def _gelu(x):
    return jax.nn.gelu(x, approximate=True)

def _silu(x):
    return jax.nn.silu(x)

def _sigmoid(x):
    return jax.nn.sigmoid(x)

def _layernorm(x, axis=-1, eps=1e-05):
    m = jnp.mean(x, axis=axis, keepdims=True)
    v = jnp.var(x, axis=axis, keepdims=True)
    return (x - m) / jnp.sqrt(v + eps)

def _scatter_add(tgt, idx, src, axis=0):
    return tgt.at[idx].add(src)

def _segment_sum(src, seg, n):
    return jax.ops.segment_sum(src, seg, n)
kernel_name = 'mk_vit_tower_cls_d1_tok_img256_r4_bac19c'

def setup_inputs(seed: int=0):
    np.random.seed(seed)
    _w = jnp.asarray

    def _rec_inputs():
        import jax
        import jax.numpy as jnp
        _rk = jax.random.key(seed)
        x = -7.10856e-05 + 0.999911 * jax.random.normal(jax.random.fold_in(_rk, 1), (8, 64, 128, 64), jnp.float32)
        cls_tok = 0.02 * jax.random.normal(jax.random.fold_in(_rk, 5), (1, 1, 64), jnp.float32)
        return (x, cls_tok)
    x, cls_tok = _rec_inputs()

    def _L0_tok_setup():
        import jax, jax.numpy as jnp
        import numpy as np
        PATCH_LEN = 16
        STRIDE = 8
        PAD = 8
        key = jax.random.key(seed)
        k1, k2 = jax.random.split(key)
        x = jax.random.normal(k1, (32, 64, 128, 64), dtype=jnp.float32)
        in_feat = 64 * (PATCH_LEN // 2 + 1) * 2
        W = jax.random.normal(k2, (64, in_feat), dtype=jnp.float32) * 0.02
        return {'x': x, 'W': W}
    _L0_tok_all = _L0_tok_setup()
    _L0_tok_in = {k: v for k, v in _L0_tok_all.items() if k in ('W',)}
    del _L0_tok_all

    def _L0_attn_setup():
        import jax, jax.numpy as jnp
        import numpy as np
        EPS = 1e-09
        key = jax.random.key(seed)
        kE, kQ, kK, kV = jax.random.split(key, 4)
        B, S, D = (8, 512, 64)
        return {'E': jax.random.normal(kE, (B, S, D), dtype=jnp.float32), 'WQ': jax.random.normal(kQ, (D, D), dtype=jnp.float32) * (1.0 / np.sqrt(D)), 'WK': jax.random.normal(kK, (D, D), dtype=jnp.float32) * (1.0 / np.sqrt(D)), 'WV': jax.random.normal(kV, (D, D), dtype=jnp.float32) * (1.0 / np.sqrt(D))}
    _L0_attn_all = _L0_attn_setup()
    _L0_attn_in = {k: v for k, v in _L0_attn_all.items() if k in ('WQ', 'WK', 'WV')}
    del _L0_attn_all

    def _L0_ffn_setup():
        import jax, jax.numpy as jnp
        import numpy as np
        BN_EPS = 0.001

        def _bn(h, g, b, m, v):
            return g * (h - m) * jax.lax.rsqrt(v + BN_EPS) + b
        key = jax.random.key(seed)
        ks = jax.random.split(key, 8)
        B, F, Df = (64, 64, 64)
        E, H, D = (8, 64, 64)
        s1 = 1.0 / np.sqrt(Df)
        s2 = 1.0 / np.sqrt(H)
        return {'x': jax.random.normal(ks[0], (B, F, Df), jnp.float32), 'Wr': jax.random.normal(ks[1], (Df, E), jnp.float32) * s1, 'br': jnp.zeros((E,), jnp.float32), 'W1': jax.random.normal(ks[2], (E, Df, H), jnp.float32) * s1, 'b1': jnp.zeros((E, H), jnp.float32), 'g1': jnp.ones((E, H), jnp.float32), 'be1': jnp.zeros((E, H), jnp.float32), 'm1': jnp.zeros((E, H), jnp.float32), 'v1': jnp.ones((E, H), jnp.float32), 'W2': jax.random.normal(ks[3], (E, H, H), jnp.float32) * s2, 'b2': jnp.zeros((E, H), jnp.float32), 'g2': jnp.ones((E, H), jnp.float32), 'be2': jnp.zeros((E, H), jnp.float32), 'm2': jnp.zeros((E, H), jnp.float32), 'v2': jnp.ones((E, H), jnp.float32), 'Wo': jax.random.normal(ks[4], (E, H, D), jnp.float32) * s2, 'bo': jnp.zeros((E, D), jnp.float32)}
    _L0_ffn_all = _L0_ffn_setup()
    _L0_ffn_in = {k: v for k, v in _L0_ffn_all.items() if k in ('Wr', 'br', 'W1', 'b1', 'g1', 'be1', 'm1', 'v1', 'W2', 'b2', 'g2', 'be2', 'm2', 'v2', 'Wo', 'bo')}
    del _L0_ffn_all
    return {'x': x, 'cls_tok': cls_tok, 'L0_tok_W': _L0_tok_in['W'], 'L0_attn_WQ': _L0_attn_in['WQ'], 'L0_attn_WK': _L0_attn_in['WK'], 'L0_attn_WV': _L0_attn_in['WV'], 'L0_ffn_Wr': _L0_ffn_in['Wr'], 'L0_ffn_br': _L0_ffn_in['br'], 'L0_ffn_W1': _L0_ffn_in['W1'], 'L0_ffn_b1': _L0_ffn_in['b1'], 'L0_ffn_g1': _L0_ffn_in['g1'], 'L0_ffn_be1': _L0_ffn_in['be1'], 'L0_ffn_m1': _L0_ffn_in['m1'], 'L0_ffn_v1': _L0_ffn_in['v1'], 'L0_ffn_W2': _L0_ffn_in['W2'], 'L0_ffn_b2': _L0_ffn_in['b2'], 'L0_ffn_g2': _L0_ffn_in['g2'], 'L0_ffn_be2': _L0_ffn_in['be2'], 'L0_ffn_m2': _L0_ffn_in['m2'], 'L0_ffn_v2': _L0_ffn_in['v2'], 'L0_ffn_Wo': _L0_ffn_in['Wo'], 'L0_ffn_bo': _L0_ffn_in['bo']}

def reference(x, cls_tok, L0_tok_W, L0_attn_WQ, L0_attn_WK, L0_attn_WV, L0_ffn_Wr, L0_ffn_br, L0_ffn_W1, L0_ffn_b1, L0_ffn_g1, L0_ffn_be1, L0_ffn_m1, L0_ffn_v1, L0_ffn_W2, L0_ffn_b2, L0_ffn_g2, L0_ffn_be2, L0_ffn_m2, L0_ffn_v2, L0_ffn_Wo, L0_ffn_bo):
    import jax
    import jax.numpy as jnp

    def _L0_tok_ref(x, W):
        import jax, jax.numpy as jnp
        import numpy as np
        PATCH_LEN = 16
        STRIDE = 8
        PAD = 8
        B, C, T, V = x.shape
        xp = jnp.pad(x, ((0, 0), (0, 0), (0, PAD), (0, 0)), mode='edge')
        Tp = T + PAD
        N = (Tp - PATCH_LEN) // STRIDE + 1
        idx = jnp.arange(N)[:, None] * STRIDE + jnp.arange(PATCH_LEN)[None, :]
        patches = xp[:, :, idx, :]
        patches = jnp.transpose(patches, (0, 4, 2, 3, 1))
        xf = jnp.fft.rfft(patches, axis=-2, norm='ortho')
        F = xf.shape[-2]
        x_real = xf.real.reshape(B, V, N, F * C)
        x_imag = xf.imag.reshape(B, V, N, F * C)
        x_emb = jnp.concatenate([x_real, x_imag], axis=-1)
        x_emb = x_emb @ W.T
        return x_emb.reshape(B, V * N, -1)

    def _L0_attn_ref(E, WQ, WK, WV):
        import jax, jax.numpy as jnp
        import numpy as np
        EPS = 1e-09
        D = E.shape[-1]
        scale = jnp.asarray(np.sqrt(D), dtype=E.dtype)
        Q = jnp.einsum('bsd,ed->bse', E, WQ)
        K = jnp.einsum('bsd,ed->bse', E, WK)
        V = jnp.einsum('bsd,ed->bse', E, WV)
        W = jnp.einsum('bqd,bkd->bqk', Q, K) / scale
        S_len = W.shape[-1]
        tril = jnp.tril(jnp.ones((S_len, S_len), dtype=W.dtype))
        M = jnp.where(W == 0, jnp.zeros_like(W), tril[None, :, :])
        x_max = jnp.max(W, axis=-1, keepdims=True)
        x_exp = jnp.exp(W - x_max) * M
        A = x_exp / (jnp.sum(x_exp, axis=-1, keepdims=True) + EPS)
        return jnp.einsum('bqk,bkd->bqd', A, V)

    def _L0_ffn_ref(x, Wr, br, W1, b1, g1, be1, m1, v1, W2, b2, g2, be2, m2, v2, Wo, bo):
        import jax, jax.numpy as jnp
        import numpy as np
        BN_EPS = 0.001

        def _bn(h, g, b, m, v):
            return g * (h - m) * jax.lax.rsqrt(v + BN_EPS) + b
        feat = jnp.mean(x, axis=0)
        w = jax.nn.softmax(feat @ Wr + br, axis=-1)
        h = jnp.einsum('bfd,edh->bfeh', x, W1) + b1
        h = jax.nn.relu(_bn(h, g1, be1, m1, v1))
        h = jnp.einsum('bfeh,ehk->bfek', h, W2) + b2
        h = jax.nn.relu(_bn(h, g2, be2, m2, v2))
        y = jnp.einsum('bfeh,ehd->bfed', h, Wo) + bo
        return jnp.einsum('bfed,fe->bfd', y, w)
    h = _L0_tok_ref(x, L0_tok_W)
    h = jnp.concatenate([jnp.broadcast_to(cls_tok, (h.shape[0], 1, h.shape[2])), h], axis=1)
    h = h + _L0_attn_ref(_layernorm(h, axis=-1), L0_attn_WQ, L0_attn_WK, L0_attn_WV)
    h = h + _L0_ffn_ref(_layernorm(h, axis=-1), L0_ffn_Wr, L0_ffn_br, L0_ffn_W1, L0_ffn_b1, L0_ffn_g1, L0_ffn_be1, L0_ffn_m1, L0_ffn_v1, L0_ffn_W2, L0_ffn_b2, L0_ffn_g2, L0_ffn_be2, L0_ffn_m2, L0_ffn_v2, L0_ffn_Wo, L0_ffn_bo)
    return h

_drawn_inputs = setup_inputs


def setup_inputs(seed=0):
    import zlib

    import numpy as np

    out = dict(_drawn_inputs(seed))
    spreads = {'L0_ffn_br': (0.0, 0.1),
     'L0_ffn_b1': (0.0, 0.1),
     'L0_ffn_g1': (1.0, 0.2),
     'L0_ffn_be1': (0.0, 0.1),
     'L0_ffn_m1': (0.0, 0.1),
     'L0_ffn_v1': (1.0, 0.2),
     'L0_ffn_b2': (0.0, 0.1),
     'L0_ffn_g2': (1.0, 0.2),
     'L0_ffn_be2': (0.0, 0.1),
     'L0_ffn_m2': (0.0, 0.1),
     'L0_ffn_v2': (1.0, 0.2),
     'L0_ffn_bo': (0.0, 0.1)}
    factors = {}
    for name, (base, spread) in spreads.items():
        noise = np.random.default_rng([zlib.crc32(name.encode()), seed]).standard_normal(out[name].shape)
        drawn = base * np.exp(spread * noise) if base else spread * noise
        out[name] = jnp.asarray(drawn.astype(out[name].dtype))
    for name, factor in factors.items():
        out[name] = (out[name] * factor).astype(out[name].dtype)
    return out
```

```python
from contextlib import ExitStack

import numpy as np

import concourse.bass as bass
from concourse import mybir

F32 = mybir.dt.float32
F32R = mybir.dt.float32r
ALU = mybir.AluOpType
ACT = mybir.ActivationFunctionType
AX = mybir.AxisListType.X

NB, C, T, V = 8, 64, 128, 64
D = 64
NTOK = 16
PATCH = 16
STEP = 8
S = V * NTOK
NT = S // 128
NF = PATCH // 2 + 1
NRI = 2 * NF
EVEN, ODD = (NF + 1) // 2, NF // 2
NEXP, NPAIR = 8, 4
CH = 512
QG = 4
SCALE = 1.0 / np.sqrt(D)
EPS_SUM = 1e-9
EPS_LN = 1e-5
EPS_BN = 1e-3


def dft_table():
    p = np.arange(PATCH)[:, None]
    f = np.arange(NF)[None, :]
    re = np.cos(2 * np.pi * p * f / PATCH) / np.sqrt(PATCH)
    im = -np.sin(2 * np.pi * p * f / PATCH) / np.sqrt(PATCH)
    im[:, [0, NF - 1]] = 0.0
    co = np.stack([re, im], 1)
    order = [(i, g) for i in range(2) for g in range(0, NF, 2)] + [(i, g) for i in range(2) for g in range(1, NF, 2)]
    flat = np.stack([co[:, i, g] for i, g in order], 1)
    out = np.zeros((128, 5, NRI))
    for half in range(2):
        for r in range(4):
            out[64 * half:64 * half + 64, r] = flat[4 * half + r]
    pad = flat[STEP:].sum(0)
    pad[2 * EVEN:] *= -1
    out[64:, 4] = pad
    return out.reshape(128, 5 * NRI).astype(np.float32)


def tower(nc, x, cls_tok, tok_W, WQ, WK, WV, Wr, br, W1, b1, g1, be1, m1, v1,
          W2, b2, g2, be2, m2, v2, Wo, bo, ident_in, dft_in, out):
    ctx = ExitStack()

    def sb(name, shape, dt=F32):
        return ctx.enter_context(nc.sbuf_tensor(name, shape, dt))

    def pb(name, shape, dt=F32):
        return ctx.enter_context(nc.psum_tensor(name, shape, dt))

    def sem(name):
        return ctx.enter_context(nc.semaphore(name))

    with ctx:
        XW = sb("XW", [128, NPAIR * (S + 128)])
        X = XW[:, 0:4096].rearrange("p (j r v) -> p j r v", j=16, r=4)
        WB = XW[:, :].rearrange("p (e s) -> p e s", e=NPAIR)
        Z = sb("Z", [128, S])
        Zv = Z[:, :].rearrange("p (v n) -> p v n", n=NTOK)
        H = sb("H", [128, NB, NT * D])
        xc = sb("xc", [128, NT, D])
        e32 = sb("e32", [128, NT, D])
        prod = sb("prod", [128, NT, 2, D])
        xc2 = sb("xc2", [128, NT, D])
        e232 = sb("e232", [128, NT, D])
        feat = sb("feat", [128, NT, D])
        ehl = [sb(f"ehl{i}", [128, NT, 2 * D], F32R) for i in range(2)]
        e2hl = sb("e2hl", [128, NT, 2 * D], F32R)
        eT = [sb(f"eT{i}", [128, S], F32R) for i in range(2)]
        Gh = sb("Gh", [128, S], F32R)
        Gl = sb("Gl", [128, S], F32R)
        EP = sb("EP", [128, 3, S])
        PTh = [sb(f"PTh{g}", [128, 4 * (g + 1), CH], F32R) for g in range(2)]
        PTl = [sb(f"PTl{g}", [128, 4 * (g + 1), CH], F32R) for g in range(2)]
        UT = sb("UT", [128, CH])
        half_m = UT
        pv = sb("pv", [128, QG, D])
        ot = sb("ot", [128, QG, D])
        E2T = sb("E2T", [128, NB, S], F32R)

        ident = sb("ident", [128, 128])
        identR = sb("identR", [128, 128], F32R)
        dft = sb("dft", [128, 5, NRI])
        Wef = sb("Wef", [128, 5, 2, D])
        AhR = sb("AhR", [128, 2, D], F32R)
        AlR = sb("AlR", [128, 2, D], F32R)
        A32 = sb("A32", [128, D])
        AT32 = sb("AT32", [64, D])
        qkv = sb("qkv", [64, 3, D])
        WVT = sb("WVT", [128, D])
        e0B = sb("e0B", [128, D])
        c0B = sb("c0B", [128, D])
        c1B = sb("c1B", [128, D])
        e0T = sb("e0T", [64, 128])
        ag = sb("ag", [128, 2, D])
        v0B = sb("v0B", [128, D])
        w00 = sb("w00", [128, 1])
        W1A = sb("W1A", [128, NEXP * D], F32R)
        W1B = sb("W1B", [128, NEXP * D], F32R)
        W2h = sb("W2h", [128, NPAIR, 128], F32R)
        W2l = sb("W2l", [128, NPAIR, 128], F32R)
        WoR = sb("WoR", [128, NPAIR, 2, D], F32R)
        Wr_s = sb("Wr_s", [64, NEXP])
        bo_s = sb("bo_s", [NEXP, D])
        brB = sb("brB", [128, NEXP])
        bn = sb("bn", [128, 5, 2, NPAIR])
        bnr = sb("bnr", [10 * NPAIR, 128])
        bn_s = sb("bn_s", [128, 2, NPAIR])
        bn_c = sb("bn_c", [128, 2, NPAIR])
        s2, c2 = bn_s[:, 1, :], bn_c[:, 1, :]
        onesf = sb("onesf", [128, 128])
        T2 = [sb(f"T2_{i}", [128, CH], F32R) for i in range(2)]
        wob = sb("wob", [128, NT + 1, D])

        negm = [sb(f"negm{i}", [128, NT]) for i in range(2)]
        rmax = sb("rmax", [128, NT])
        rsum = [sb(f"rsum{i}", [128, NT]) for i in range(2)]
        sr = [sb(f"sr{i}", [128, NT, 2]) for i in range(2)]
        r0max = sb("r0max", [128, NB])
        st = sb("st", [128, 4, NT])
        st2 = sb("st2", [128, 4, NT])
        pz = sb("pz", [128, 5, QG])
        cst = sb("cst", [128, 16])
        gl9 = sb("gl9", [128, 9, NEXP])
        gw9 = sb("gw9", [128, 9, NEXP])
        gs9 = sb("gs9", [128, 3, 9])
        f64 = sb("f64", [64, 128])
        clsS = sb("clsS", [8, 16])
        h2c = sb("h2c", [8, D])
        ccx = sb("ccx", [8, D])
        e2c = sb("e2c", [8, D])
        e2cR = sb("e2cR", [8, 2 * D], F32R)
        e2cT = sb("e2cT", [128, 8], F32R)
        Oc = sb("Oc", [8, D])

        Hs = H[:, 2:8, :].rearrange("p b n -> p (b n)")
        dgs, dgc, s1B, b1B, g1B, W1raw = (Hs[:, CH * i:CH * (i + 1)] for i in range(6))
        EPs = EP[:, :, :].rearrange("p a n -> p (a n)")
        W2raw = EPs[:, 0:512].rearrange("p (a n) -> p a n", a=NPAIR)
        Woraw = EPs[:, 512:768].rearrange("p (a n) -> p a n", a=NPAIR)
        Wraw = EPs[0:64, 768:768 + NRI * C].rearrange("p (g c) -> p g c", c=C)
        WTe = EPs[:, 1920:1920 + 640].rearrange("p (d g) -> p d g", d=D)
        WTo = EPs[:, 2560:2560 + 512].rearrange("p (d g) -> p d g", d=D)
        prE = prod[:, :, :, :].rearrange("p a b c -> p (a b c)")[:, 0:640].rearrange("p (d g) -> p d g", d=D)
        prO = Z[:, 0:512].rearrange("p (d g) -> p d g", d=D)
        sumE = e232[:, 0:5, :]
        sumO = xc2[:, 0:5, :]

        h1h = [PTh[1][:, 4 * i:4 * i + 4, :] for i in range(2)]
        h1l = [PTl[1][:, 4 * i:4 * i + 4, :] for i in range(2)]
        th, tl = PTh[0], PTl[0]
        r2 = EPs[:, 0:2048].rearrange("p (a n) -> p a n", a=NPAIR)
        t2 = Z[:, 0:1024].rearrange("p (a n) -> p a n", a=2)
        FT = Z[0:64, :]
        wT = EPs[0:NEXP, 0:9 * 128]
        gx = [EPs[:, 1152:2176].rearrange("p (t n) -> p t n", t=NT), prod[:, :, :, :].rearrange("p t s d -> p t (s d)")]
        gx8 = xc2[:, :, :].rearrange("p t d -> p (t d)").rearrange("p (a n) -> p a n", a=NPAIR)
        O32 = [xc[:, QG * i:QG * i + QG, :] for i in range(2)]
        yT = UT

        Sp = [pb(f"Sp{i}", [128, 2 * CH]) for i in range(2)]
        PTp = [pb(f"PTp{i}", [128, CH]) for i in range(2)]
        M0 = pb("M0", [128, CH])
        M1 = pb("M1", [128, CH])
        L1p = [Sp[0][:, 0:CH], Sp[0][:, CH:2 * CH], Sp[1][:, 0:CH], Sp[1][:, CH:2 * CH]]
        L2p = [PTp[0], PTp[1]]

        ld_first, ld_w, ld_x, ld_ffn, ld_bn, st_cls = (
            sem(n) for n in "ld_first ld_w ld_x ld_ffn ld_bn st_cls".split())
        wt_copied, evn_mul, evn_sum, odd_mul, odd_sum = (
            sem(n) for n in "wt_copied evn_mul evn_sum odd_mul odd_sum".split())
        y_ready, z_done, zt_ready, ha_done, h_done = (
            sem(n) for n in "y_ready z_done zt_ready ha_done h_done".split())
        n1_sum, n1_mean, n1_cent, n1_sq, n1_ss, n1_var, n1_rstd = (
            sem(n) for n in "n1_sum n1_mean n1_cent n1_sq n1_ss n1_var n1_rstd".split())
        e_done, eh_done, el_done, prod_done, sr_done, r0_done = (
            sem(n) for n in "e_done eh_done el_done prod_done sr_done r0_done".split())
        et_ready, et_done, g_ready, gh_done, gl_done = (
            sem(n) for n in "et_ready et_done g_ready gh_done gl_done".split())
        s_ready, max_done, negm_done, exp_done, tri_done, p_done, pt_ready, pth_done, ptl_done = (
            sem(n) for n in "s_ready max_done negm_done exp_done tri_done p_done pt_ready pth_done ptl_done".split())
        u_ready, u_done, o_ready, p0_arg, p0_exp, p0_done, tot_done, rinv_done = (
            sem(n) for n in "u_ready u_done o_ready p0_arg p0_exp p0_done tot_done rinv_done".split())
        a0_done, ot_done, pv_done, pvs_done, h2_done = (
            sem(n) for n in "a0_done ot_done pv_done pvs_done h2_done".split())
        n2_sum, n2_mean, n2_cent, n2_sq, n2_ss, n2_var, n2_rstd = (
            sem(n) for n in "n2_sum n2_mean n2_cent n2_sq n2_ss n2_var n2_rstd".split())
        e2_done, e2h_done, e2l_done, feat_done, e2t_ready, e2t_done = (
            sem(n) for n in "e2_done e2h_done e2l_done feat_done e2t_ready e2t_done".split())
        passed_pool, passed_dve = (
            sem(n) for n in "passed_pool passed_dve".split())
        t2_done, l1_ready, h1h_done, h1l_done, l2_ready, r_done, t_done, th_done, tl_done = (
            sem(n) for n in "t2_done l1_ready h1h_done h1l_done l2_ready r_done t_done th_done tl_done".split())
        l3_ready, y_done, tr_ready, oa_done, o_done, hw_done = (
            sem(n) for n in "l3_ready y_done tr_ready oa_done o_done hw_done".split())
        st_half = [sem(f"st_half{c}") for c in range(2)]
        once = {
            "pool_steps": """const_set const_set const_set bn_z const_set c_var c_rstd bn_var bn_m bn_rstd bn_scale bn_ms bn_shift
                bn_diag bn_diag bn_w1 bn_w1l bn_bl bn_w2l bn_wol t2_rows
                k_h1 k_h2 k_var k_rstd k_el""".split(),
            "act_steps": """a_copied a_copied a_copied bn_Tc ah_done ah_done c_sq c_e0Tc c_vecc c_vecc
                bn_row bn_row bn_w1h bn_b32 bn_bh bn_w2 bn_wo t2_set t2_set
                k_exp k_sq k_eh k_eTc q_fc q_fc q_cmc q_exp q_wTc q_wTc q_wTc q_bcc q_bcc q_bcc q_bcc q_bcc""".split(),
            "dve_steps": """tabR c_sum c_mean c_cent wef_done wef_done al_done al_done c_ss c_e0 c_w00p c_w00
                k_max k_max2 k_neg k_p0 k_tot k_rc k_a0 k_sum k_mean k_cent k_ss k_e2
                q_lgb q_mx q_sub q_sum q_rc q_w q_gx q_gx q_gx q_gx q_gx q_wbc""".split(),
            "pe_steps": """wraw_T wraw_T wraw_T bn_T a_ready c_e0T c_vec bn_rows bn_rows k_r0T q_fT q_fT k_eT q_cm q_lg
                q_wT q_wT q_wT q_bc q_bc q_bc q_bc q_bc q_wb""".split(),
        }
        pool_steps, act_steps, dve_steps, pe_steps = (sem(engine) for engine in once)

        def nth(step, n):
            engine, = (steps for steps in once.values() if step in steps)
            return [0, *(place + 1 for place, name in enumerate(engine) if name == step)][max(n, 0)]

        def at(value):
            return max(value, 0) if isinstance(value, int) else value


        def bc(ap, n):
            return ap.unsqueeze(2).to_broadcast([ap.shape[0], ap.shape[1], n])

        def bct(ap, n):
            return ap.unsqueeze(1).to_broadcast([ap.shape[0], n, ap.shape[1]])

        def Hb(b, t0=0, n=NT):
            return H[:, bass.ds(b, 1), t0 * D:(t0 + n) * D].rearrange("p a (t d) -> p (a t) d", d=D)

        def chunks(t):
            if t < QG:
                return [(t, 0, t + 1)]
            return [(QG + 2 * (t - QG), 0, QG), (QG + 2 * (t - QG) + 1, QG, t - QG + 1)]

        NCH = 12

        block = ctx.enter_context(nc.Block())

        @block.sync
        def _(sp):
            sp.dma_start(Wraw, tok_W.rearrange("d (g c) -> d g c", c=C)).then_inc(ld_first, 16)
            sp.dma_start(dft[:, :, :], dft_in.rearrange("p (r g) -> p r g", r=5)).then_inc(ld_first, 16)
            sp.dma_start(ident[:, :], ident_in).then_inc(ld_first, 16)
            for n, src in enumerate((WQ, WK, WV)):
                sp.dma_start(qkv[:, n, :], src).then_inc(ld_w, 16)
            sp.dma_start(c0B[:, :], cls_tok[0, :, :].to_broadcast([128, D])).then_inc(ld_w, 16)
            for n, src in enumerate((g1, g2, v1, v2, b1, b2, m1, m2, be1, be2)):
                sp.dma_start(bnr[NPAIR * n:NPAIR * n + NPAIR, :], src.rearrange("(a s) k -> a (s k)", s=2)).then_inc(ld_bn, 16)

            def load_x(b):
                sp.wait_ge(y_ready, at(3 * b))
                for half in range(2):
                    src = x[bass.ds(b, 1), :, :, :].rearrange("a c (j h r) v -> (a c) j h (r v)", h=2, r=4)
                    sp.dma_start(X[64 * half:64 * half + 64, :, :, :].rearrange("p j r v -> p j (r v)"),
                                 src[:, :, half, :]).then_inc(ld_x, 16)

            load_x(0)
            for half in range(2):
                sp.dma_start(W1raw[64 * half:64 * half + 64, :].rearrange("p (e h) -> p e h", e=NEXP),
                               W1.rearrange("e d h -> d e h")).then_inc(ld_ffn, 16)
            sp.wait_ge(pool_steps, nth("bn_z", 1))
            for half in range(2):
                sp.dma_start(W2raw[64 * half:64 * half + 64, :, 64 * half:64 * half + 64],
                               W2.rearrange("(a s) h k -> s h a k", s=2)[half, :, :, :]).then_inc(ld_ffn, 16)
            for half in range(2):
                sp.dma_start(Woraw[64 * half:64 * half + 64, :, :],
                               Wo.rearrange("(a s) h k -> s h a k", s=2)[half, :, :, :]).then_inc(ld_ffn, 16)
            sp.dma_start(Wr_s[:, :], Wr).then_inc(ld_ffn, 16)
            sp.dma_start(bo_s[:, :], bo).then_inc(ld_ffn, 16)
            sp.dma_start(brB[:, :], br.rearrange("(a e) -> a e", a=1).to_broadcast([128, NEXP])).then_inc(ld_ffn, 16)
            with sp.Fori(1, NB) as b:
                load_x(b)

            def store(k, b, c):
                sp.wait_ge(o_done, at(k + 1))
                dst = out[bass.ds(b, 1), 1 + CH * c:1 + CH * (c + 1), :].rearrange("a (t p) d -> p (a t) d", p=128)
                sp.dma_start(dst, O32[c][:, :, :]).then_inc(st_half[c], 16)

            with sp.Fori(0, NB) as b:
                store(2 * b, b, 0)
                store(2 * b + 1, b, 1)
            sp.wait_ge(o_done, at(2 * NB + 1))
            sp.dma_start(out[:, 0, :], Oc[:, :]).then_inc(st_cls, 16)
            sp.wait_ge(st_half[0], at(16 * NB))
            sp.wait_ge(st_half[1], at(16 * NB))
            sp.wait_ge(st_cls, 16)

        @block.gpsimd
        def _(pool):
            pool.memset(half_m[:, :], -0.5).then_inc(pool_steps, 1)
            pool.memset(onesf[:, :], 1.0).then_inc(pool_steps, 1)
            pool.memset(cst[:, :], 1.0 / NB).then_inc(pool_steps, 1)
            pool.memset(EPs[:, 0:512], 0.0).then_inc(pool_steps, 1)
            pool.wait_ge(pool_steps, nth("const_set", 3))
            pool.memset(cst[:, 8:16], -0.5).then_inc(pool_steps, 1)
            pool.memset(feat[:, :, :], 0.0).then_inc(feat_done, 1)
            pool.wait_ge(ld_first, 48)
            pool.wait_ge(wt_copied, 3)
            for r in range(5):
                pool.wait_ge(odd_sum, at(r))
                pool.tensor_tensor(prO, WTo, bct(dft[:, r, 2 * EVEN:NRI], D), ALU.mult).then_inc(odd_mul, 1)
            pool.wait_ge(dve_steps, nth("c_ss", 1))
            pool.tensor_scalar(st[:, 2, 0:1], st[:, 1, 0:1], 1.0 / D, EPS_LN, ALU.mult, ALU.add).then_inc(pool_steps, 1)
            pool.wait_ge(pool_steps, nth("c_var", 1))
            pool.wait_ge(pool_steps, nth("const_set", 1))
            pool.tensor_tensor(st[:, 3, 0:1], st[:, 2, 0:1], half_m[:, 0:1], ALU.pow).then_inc(pool_steps, 1)

            pool.wait_ge(act_steps, nth("bn_Tc", 1))
            pool.tensor_scalar(bn[:, 1, :, :], bn[:, 1, :, :], 1.0, EPS_BN, ALU.mult, ALU.add).then_inc(pool_steps, 1)
            pool.tensor_tensor(bn[:, 2, :, :], bn[:, 2, :, :], bn[:, 3, :, :], ALU.subtract).then_inc(pool_steps, 1)
            pool.wait_ge(pool_steps, nth("bn_var", 1))
            pool.tensor_tensor(bn[:, 1, :, :], bn[:, 1, :, :], half_m[:, 0:2 * NPAIR].rearrange("p (l a) -> p l a", l=2),
                               ALU.pow).then_inc(pool_steps, 1)
            pool.wait_ge(pool_steps, nth("bn_rstd", 1))
            pool.tensor_tensor(bn_s[:, :, :], bn[:, 1, :, :], bn[:, 0, :, :], ALU.mult).then_inc(pool_steps, 1)
            pool.wait_ge(pool_steps, nth("bn_scale", 1))
            pool.tensor_tensor(bn[:, 2, :, :], bn[:, 2, :, :], bn_s[:, :, :], ALU.mult).then_inc(pool_steps, 1)
            pool.wait_ge(pool_steps, nth("bn_ms", 1))
            pool.tensor_tensor(bn_c[:, :, :], bn[:, 2, :, :], bn[:, 4, :, :], ALU.add).then_inc(pool_steps, 1)
            pool.wait_ge(pool_steps, nth("bn_shift", 1))
            for dst, col in ((dgs, bn_s), (dgc, bn_c)):
                pool.tensor_tensor(dst.rearrange("p (a n) -> p a n", a=NPAIR), bct(ident[:, :], NPAIR), bc(col[:, 0, :], 128),
                                   ALU.mult).then_inc(pool_steps, 1)

            def ln1_rstd(b):
                pool.wait_ge(n1_ss, at(b + 1))
                pool.sem_inc(passed_pool)
                pool.tensor_scalar(st[:, 2, :], st[:, 1, :], 1.0 / D, EPS_LN, ALU.mult, ALU.add).then_inc(n1_var, 1)
                pool.wait_ge(n1_var, at(b + 1))
                pool.sem_inc(passed_pool)
                pool.tensor_tensor(st[:, 3, :], st[:, 2, :], cst[:, 8:8 + NT], ALU.pow).then_inc(n1_rstd, 1)

            def ln1_low(b, q):
                pool.wait_ge(eh_done, at(b + 1))
                pool.sem_inc(passed_pool)
                pool.tensor_tensor(ehl[q][:, :, D:2 * D], e32[:, :, :], ehl[q][:, :, 0:D].bitcast(F32),
                                   ALU.subtract).then_inc(el_done, 1)

            def ln1_prod(b):
                pool.wait_ge(act_steps, nth("c_vecc", 2))
                pool.wait_ge(e_done, at(b + 1))
                pool.sem_inc(passed_pool)
                pool.wait_ge(sr_done, at(b))
                pool.sem_inc(passed_pool)
                pool.tensor_tensor(prod[:, :, :, :],
                                   e32[:, :, :].unsqueeze(2).to_broadcast([128, NT, 2, D]),
                                   ag[:, :, :].unsqueeze(1).to_broadcast([128, NT, 2, D]),
                                   ALU.mult).then_inc(prod_done, 1)

            def tri(b, t):
                pool.wait_ge(exp_done, at(8 * b + t + 1))
                pool.sem_inc(passed_pool)
                blk_ = EP[:, t % 2, 128 * t:128 * t + 128]
                pool.affine_select(out=blk_, in_=blk_, compare_op=ALU.is_ge, fill=0.0, base=0,
                                   pattern=[[-1, 128]], channel_multiplier=1).then_inc(tri_done, 1)

            def add_rest(b, g):
                pool.wait_ge(a0_done, at(2 * b + g + 1))
                pool.sem_inc(passed_pool)
                pool.tensor_tensor(pv[:, :, :], bc(pz[:, 4, :], D), bct(v0B[:, :], QG), ALU.mult).then_inc(pv_done, 1)
                pool.wait_ge(pv_done, at(2 * b + g + 1))
                pool.sem_inc(passed_pool)
                hb = Hb(b, QG * g, QG)
                pool.tensor_tensor(hb, hb, pv[:, :, :], ALU.add).then_inc(pvs_done, 1)
                pool.wait_ge(ot_done, at(2 * b + g + 1))
                pool.sem_inc(passed_pool)
                pool.wait_ge(pvs_done, at(2 * b + g + 1))
                pool.sem_inc(passed_pool)
                pool.tensor_tensor(hb, hb, ot[:, :, :], ALU.add).then_inc(h2_done, 1)

            def ln2_rstd(b):
                pool.wait_ge(n2_ss, at(b + 1))
                pool.sem_inc(passed_pool)
                pool.tensor_scalar(st2[:, 2, :], st2[:, 1, :], 1.0 / D, EPS_LN, ALU.mult, ALU.add).then_inc(n2_var, 1)
                pool.wait_ge(n2_var, at(b + 1))
                pool.sem_inc(passed_pool)
                pool.tensor_tensor(st2[:, 3, :], st2[:, 2, :], cst[:, 8:8 + NT], ALU.pow).then_inc(n2_rstd, 1)

            def ln2_low(b):
                pool.wait_ge(e2h_done, at(b + 1))
                pool.sem_inc(passed_pool)
                pool.tensor_tensor(e2hl[:, :, D:2 * D], e232[:, :, :], e2hl[:, :, 0:D].bitcast(F32),
                                   ALU.subtract).then_inc(e2l_done, 1)
                pool.wait_ge(feat_done, at(b + 1))
                pool.sem_inc(passed_pool)
                pool.tensor_tensor(feat[:, :, :], feat[:, :, :], e232[:, :, :], ALU.add).then_inc(feat_done, 1)

            pool.wait_ge(ld_ffn, 16 * 9)
            pool.wait_ge(act_steps, nth("bn_row", 1))
            pool.tensor_tensor(W1raw, W1raw, s1B, ALU.mult).then_inc(pool_steps, 1)
            pool.wait_ge(pool_steps, nth("const_set", 4))
            ln1_rstd(0)
            pool.wait_ge(act_steps, nth("bn_w1h", 1))
            pool.tensor_tensor(W1B[0:64, :], W1raw[0:64, :], W1A[0:64, :].bitcast(F32), ALU.subtract).then_inc(pool_steps, 1)
            pool.wait_ge(pool_steps, nth("bn_w1l", 1))
            pool.wait_ge(act_steps, nth("bn_bh", 1))
            pool.tensor_tensor(W1B[96:128, :], b1B[96:128, :], g1B[96:128, :], ALU.subtract).then_inc(pool_steps, 1)
            pool.wait_ge(pool_steps, nth("bn_bl", 1))
            ln1_low(0, 0)
            ln1_prod(0)
            pool.wait_ge(act_steps, nth("bn_w2", 1))
            pool.tensor_tensor(W2l[:, :, :], W2raw, W2h[:, :, :].bitcast(F32), ALU.subtract).then_inc(pool_steps, 1)
            pool.wait_ge(act_steps, nth("bn_wo", 1))
            pool.tensor_tensor(WoR[:, :, 1, :], Woraw, WoR[:, :, 0, :].bitcast(F32), ALU.subtract).then_inc(pool_steps, 1)
            pool.wait_ge(pool_steps, nth("bn_wol", 1))
            pool.tensor_scalar(half_m[64:128, :], half_m[64:128, :], -1.0 / 16, 0.0, ALU.mult, ALU.add).then_inc(pool_steps, 1)
            tri(0, 0)

            def body(b, q, first=False, last=False):
                for t in range(NT):
                    if t < NT - 1:
                        tri(b, t + 1)
                    elif not last:
                        tri(b + 1, 0)
                    if not first:
                        if t == 2:
                            add_rest(b - 1, 1)
                        if t == 5:
                            ln2_rstd(b - 1)
                        if t == 6:
                            ln2_low(b - 1)
                    if not last:
                        if t == 4:
                            ln1_rstd(b + 1)
                        if t == 5:
                            ln1_low(b + 1, 1 - q)
                            ln1_prod(b + 1)
                    if t == 6:
                        add_rest(b, 0)

            body(0, 0, first=True)
            with pool.Fori(0, NB // 2 - 1) as j:
                body(2 * j + 1, 1)
                body(2 * j + 2, 0)
            body(NB - 1, 1, last=True)
            add_rest(NB - 1, 1)
            ln2_rstd(NB - 1)
            ln2_low(NB - 1)

            pool.wait_ge(dve_steps, nth("k_a0", 1))
            pool.tensor_tensor(ccx[:, :], v0B[0:8, :], clsS[:, 6:7].to_broadcast([8, D]), ALU.mult).then_inc(pool_steps, 1)
            pool.wait_ge(pool_steps, nth("k_h1", 1))
            pool.tensor_tensor(h2c[:, :], ccx[:, :], c0B[0:8, :], ALU.add).then_inc(pool_steps, 1)
            pool.wait_ge(dve_steps, nth("k_ss", 1))
            pool.tensor_scalar(clsS[:, 10:11], clsS[:, 9:10], 1.0 / D, EPS_LN, ALU.mult, ALU.add).then_inc(pool_steps, 1)
            pool.wait_ge(pool_steps, nth("k_var", 1))
            pool.tensor_tensor(clsS[:, 11:12], clsS[:, 10:11], cst[0:8, 8:9], ALU.pow).then_inc(pool_steps, 1)
            pool.wait_ge(act_steps, nth("k_eh", 1))
            pool.tensor_tensor(e2cR[:, D:2 * D], e2c[:, :], e2cR[:, 0:D].bitcast(F32), ALU.subtract).then_inc(pool_steps, 1)

            def low(k, p):
                pool.wait_ge(th_done, at(4 * k + p + 1))
                pool.sem_inc(passed_pool)
                pool.wait_ge(l3_ready, at(k))
                pool.sem_inc(passed_pool)
                pool.tensor_tensor(tl[:, p, :], t2[:, p % 2, :], th[:, p, :].bitcast(F32), ALU.subtract).then_inc(tl_done, 1)

            def resid(b, c):
                hb = Hb(b, QG * c, QG)
                pool.tensor_tensor(hb, hb, wob[:, QG * c:QG * c + QG, :], ALU.add).then_inc(hw_done, 1)

            pool.wait_ge(dve_steps, nth("q_wbc", 1))

            def chunk_pair(b):
                for c in range(2):
                    low(2 * b + c, 0)
                    low(2 * b + c, 1)
                    resid(b, c)
                    low(2 * b + c, 2)
                    low(2 * b + c, 3)

            chunk_pair(0)
            with pool.Fori(1, NB) as b:
                chunk_pair(b)
            for p in range(NPAIR):
                pool.wait_ge(th_done, at(8 * NB + p + 1))
                pool.sem_inc(passed_pool)
                pool.wait_ge(l3_ready, at(2 * NB))
                pool.sem_inc(passed_pool)
                pool.tensor_tensor(tl[:, p, 0:8], t2[:, p % 2, 0:8], th[:, p, 0:8].bitcast(F32), ALU.subtract).then_inc(tl_done, 1)
            pool.tensor_tensor(h2c[:, :], h2c[:, :], wob[0:8, NT, :], ALU.add).then_inc(hw_done, 1)

        @block.scalar
        def _(act):
            def copy(dst, src):
                return act.activation(dst, src, ACT.Copy)

            for n in range(3):
                act.wait_ge(pe_steps, nth("wraw_T", n + 1))
                if n < 2:
                    src = Sp[n][:, 0:CH] if n == 0 else Sp[1][:, 0:CH]
                if n == 0:
                    copy(WTe[:, :, 0:5], Sp[0][:, 0:5 * D].rearrange("p (g d) -> p d g", d=D)).then_inc(wt_copied, 1)
                elif n == 1:
                    copy(WTe[:, :, 5:10], Sp[0][:, CH:CH + 5 * D].rearrange("p (g d) -> p d g", d=D)).then_inc(wt_copied, 1)
                else:
                    copy(WTo, Sp[1][:, 0:8 * D].rearrange("p (g d) -> p d g", d=D)).then_inc(wt_copied, 1)
            act.wait_ge(pe_steps, nth("a_ready", 1))
            copy(A32[:, :], M1[:, 0:D]).then_inc(act_steps, 1)
            copy(AT32[:, :], M1[0:64, D:2 * D]).then_inc(act_steps, 1)
            copy(WVT[:, :], M1[:, 2 * D:3 * D]).then_inc(act_steps, 1)
            copy(bn[:, :, :, :], M1[:, 320:360].rearrange("p (n l a) -> p n l a", n=5, l=2)).then_inc(act_steps, 1)
            act.wait_ge(act_steps, nth("a_copied", 1))
            for i in range(2):
                copy(AhR[:, i, :], A32[:, :]).then_inc(act_steps, 1)
            act.wait_ge(dve_steps, nth("c_cent", 1))
            act.activation(e0B[:, :], c1B[:, :], ACT.Square).then_inc(act_steps, 1)
            act.wait_ge(pe_steps, nth("c_e0T", 1))
            copy(e0T[:, :], M1[0:64, 3 * D:3 * D + 128]).then_inc(act_steps, 1)
            act.wait_ge(pe_steps, nth("c_vec", 1))
            copy(ag[:, :, :], M1[:, 0:2 * D].rearrange("p (a d) -> p a d", a=2)).then_inc(act_steps, 1)
            copy(v0B[:, :], M1[:, 2 * D:3 * D]).then_inc(act_steps, 1)

            def z_copy(b, n):
                act.wait_ge(y_ready, at(3 * b + n + 1))
                if n == 0:
                    act.wait_ge(zt_ready, at(2 * b))
                if n < 2:
                    y = M0[:, :].rearrange("p (j v) -> p v j", j=8)
                    copy(Zv[0:64, :, 8 * n:8 * n + 8], y[0:64, :, :])
                    lo = 1 - n
                    copy(Zv[64:128, :, 8 * n - 1 + lo:8 * n + 7], y[64:128, :, lo:8]).then_inc(z_done, 1)
                else:
                    copy(Zv[64:128, :, NTOK - 1], M0[64:128, 0:V]).then_inc(z_done, 1)

            def h_first(b, c):
                act.wait_ge(zt_ready, at(2 * b + c + 1))
                copy(Hb(b, QG * c, QG), (M0, M1)[c][:, :].rearrange("p (t s d) -> p t s d", s=2, d=D)[:, :, 0, :])\
                    .then_inc(ha_done, 1)

            def ln1_sq(b):
                act.wait_ge(n1_cent, at(b + 1))
                act.wait_ge(prod_done, at(b))
                act.activation(e32[:, :, :], xc[:, :, :], ACT.Square).then_inc(n1_sq, 1)

            def ln1_high(b, q):
                act.wait_ge(e_done, at(b + 1))
                act.wait_ge(u_ready, at(2 * (b - 1)))
                copy(ehl[q][:, :, 0:D], e32[:, :, :]).then_inc(eh_done, 1)

            def et_copy(b, q, c):
                act.wait_ge(et_ready, at(2 * b + c + 1))
                copy(eT[q][:, CH * c:CH * c + CH], M0[:, :]).then_inc(et_done, 1)

            def gh(b, c):
                act.wait_ge(g_ready, at(2 * b + c + 1))
                act.wait_ge(s_ready, at(8 * (b - 1) + 4 * c + 4))
                copy(Gh[:, CH * c:CH * c + CH], M0[:, :]).then_inc(gh_done, 1)

            def expo(b, q, t):
                act.wait_ge(negm_done, at(8 * b + t + 1))
                act.wait_ge(p_done, at(8 * b + t - 1))
                n = 128 * (t + 1)
                act.activation(EP[:, t % 2, 0:n], Sp[t % 2][:, 0:n], ACT.Exp, bias=negm[q][:, t:t + 1],
                               scale=SCALE).then_inc(exp_done, 1)

            def pth(b, t):
                for i, k0, n in chunks(t):
                    act.wait_ge(pt_ready, at(NCH * b + i + 1))
                    g, tq = t // QG, t % QG
                    if tq == 0:
                        act.wait_ge(u_ready, at(2 * (b - 1) + g + 1))
                    copy(PTh[g][:, k0:k0 + n, 128 * tq:128 * tq + 128],
                         PTp[i % 2][:, 0:128 * n].rearrange("p (k q) -> p k q", q=128)).then_inc(pth_done, 1)

            def u_copy(b, g):
                act.wait_ge(u_ready, at(2 * b + g + 1))
                act.wait_ge(o_ready, at(2 * b + g))
                copy(UT[:, :], M1[:, :]).then_inc(u_done, 1)

            def class_exp(b, g):
                act.wait_ge(p0_arg, at(2 * b + g + 1))
                act.activation(pz[:, 1, :], pz[:, 0, :], ACT.Exp).then_inc(p0_exp, 1)

            def ln2_sq(b):
                act.wait_ge(n2_cent, at(b + 1))
                act.wait_ge(feat_done, at(b + 1))
                act.activation(e232[:, :, :], xc2[:, :, :], ACT.Square).then_inc(n2_sq, 1)

            def ln2_high(b):
                act.wait_ge(e2_done, at(b + 1))
                copy(e2hl[:, :, 0:D], e232[:, :, :]).then_inc(e2h_done, 1)

            def e2t_copy(b, c):
                act.wait_ge(e2t_ready, at(2 * b + c + 1))
                copy(E2T[:, bass.ds(b, 1), CH * c:CH * c + CH], M1[:, :].unsqueeze(1)).then_inc(e2t_done, 1)

            for n in range(3):
                z_copy(0, n)
            h_first(0, 0)
            h_first(0, 1)
            for n, dst in enumerate((s1B, b1B)):
                act.wait_ge(pe_steps, nth("bn_rows", n + 1))
                copy(dst, PTp[n][:, :]).then_inc(act_steps, 1)
            ln1_sq(0)
            act.wait_ge(pool_steps, nth("bn_w1", 1))
            copy(W1A[:, :], W1raw).then_inc(act_steps, 1)
            act.wait_ge(act_steps, nth("bn_row", 2))
            copy(W1B[64:96, :], b1B[64:96, :])
            copy(T2[0][96:128, :], b1B[96:128, :]).then_inc(act_steps, 1)
            act.wait_ge(act_steps, nth("bn_b32", 1))
            copy(g1B[96:128, :], T2[0][96:128, :].bitcast(F32)).then_inc(act_steps, 1)
            ln1_high(0, 0)
            copy(W2h[:, :, :], W2raw).then_inc(act_steps, 1)
            copy(WoR[:, :, 0, :], Woraw).then_inc(act_steps, 1)
            et_copy(0, 0, 0)
            et_copy(0, 0, 1)
            gh(0, 0)
            gh(0, 1)
            act.wait_ge(pool_steps, nth("t2_rows", 1))
            act.wait_ge(act_steps, nth("bn_bh", 1))
            for i in range(2):
                copy(T2[i][64:128, :], half_m[64:128, :]).then_inc(act_steps, 1)
            expo(0, 0, 0)

            def body(b, q, first=False, last=False):
                for t in range(NT):
                    if t > 0:
                        pth(b, t - 1)
                    elif not first:
                        pth(b - 1, NT - 1)
                    if t < NT - 1:
                        expo(b, q, t + 1)
                    elif not last:
                        expo(b + 1, 1 - q, 0)
                    if not first:
                        if t == 1:
                            class_exp(b - 1, 1)
                            u_copy(b - 1, 1)
                        if t == 4:
                            ln2_sq(b - 1)
                        if t == 6:
                            ln2_high(b - 1)
                        if t == 7:
                            e2t_copy(b - 1, 0)
                            e2t_copy(b - 1, 1)
                    if t == 5:
                        class_exp(b, 0)
                        u_copy(b, 0)
                    if not last:
                        if t == (1 if first else 0):
                            z_copy(b + 1, 0)
                        if t == 2:
                            z_copy(b + 1, 1)
                            z_copy(b + 1, 2)
                            h_first(b + 1, 0)
                            h_first(b + 1, 1)
                        if t == 3:
                            ln1_sq(b + 1)
                        if t == 5:
                            ln1_high(b + 1, 1 - q)
                            et_copy(b + 1, 1 - q, 0)
                        if t == 6:
                            et_copy(b + 1, 1 - q, 1)
                            gh(b + 1, 0)
                            gh(b + 1, 1)

            body(0, 0, first=True)
            with act.Fori(0, NB // 2 - 1) as j:
                body(2 * j + 1, 1)
                body(2 * j + 2, 0)
            body(NB - 1, 1, last=True)
            b = NB - 1
            pth(b, NT - 1)
            u_copy(b, 1)
            class_exp(b, 1)
            act.wait_ge(dve_steps, nth("k_neg", 1))
            act.activation(clsS[:, 3:4], clsS[:, 2:3], ACT.Exp).then_inc(act_steps, 1)
            ln2_sq(b)
            ln2_high(b)
            e2t_copy(b, 0)
            e2t_copy(b, 1)

            act.wait_ge(dve_steps, nth("k_cent", 1))
            act.activation(e2c[:, :], ccx[:, :], ACT.Square).then_inc(act_steps, 1)
            act.wait_ge(dve_steps, nth("k_e2", 1))
            copy(e2cR[:, 0:D], e2c[:, :]).then_inc(act_steps, 1)
            act.wait_ge(pe_steps, nth("k_eT", 1))
            copy(e2cT[:, :], M1[:, 0:8]).then_inc(act_steps, 1)
            for c in range(2):
                act.wait_ge(pe_steps, nth("q_fT", c + 1))
                act.activation(FT[:, CH * c:CH * c + CH], Sp[0][0:64, CH * c:CH * c + CH], ACT.Copy, scale=1.0 / NB)\
                    .then_inc(act_steps, 1)
            act.wait_ge(pe_steps, nth("q_cm", 1))
            copy(f64[:, :], Sp[1][0:64, CH:CH + 128]).then_inc(act_steps, 1)
            act.wait_ge(dve_steps, nth("q_sub", 1))
            act.activation(gl9[:, :, :], gl9[:, :, :], ACT.Exp).then_inc(act_steps, 1)
            for c in range(3):
                act.wait_ge(pe_steps, nth("q_wT", c + 1))
                n = QG if c < 2 else 1
                copy(wT[:, CH * c:CH * c + 128 * n], PTp[c % 2][0:8, 0:128 * n]).then_inc(act_steps, 1)
            for i in range(NPAIR):
                act.wait_ge(pe_steps, nth("q_bc", i + 1))
                copy(WB[:, i, 0:S], Sp[i % 2][:, :]).then_inc(act_steps, 1)
            act.wait_ge(pe_steps, nth("q_bc", NPAIR + 1))
            copy(WB[:, :, S:S + 128], M0[:, :].rearrange("p (e s) -> p e s", e=NPAIR)).then_inc(act_steps, 1)

            def h1_high(k, q, p, n=CH):
                act.wait_ge(l1_ready, at(4 * k + p + 1))
                act.wait_ge(l2_ready, at(4 * (k - 2) + p + 1))
                act.activation(h1h[q][:, p, 0:n], L1p[p][:, 0:n], ACT.Relu).then_inc(h1h_done, 1)

            def r_act(k, p, n=CH):
                act.wait_ge(l2_ready, at(4 * k + p + 1))
                act.wait_ge(t_done, at(4 * k + p - 3))
                act.activation(r2[:, p, 0:n], L2p[p % 2][:, 0:n], ACT.Relu, bias=c2[:, p:p + 1],
                               scale=s2[:, p:p + 1]).then_inc(r_done, 1)

            def t_high(k, p, n=CH):
                act.wait_ge(t_done, at(4 * k + p + 1))
                act.wait_ge(l3_ready, at(k))
                copy(th[:, p, 0:n], t2[:, p % 2, 0:n]).then_inc(th_done, 1)

            def y_copy(k, n=CH):
                act.wait_ge(l3_ready, at(k + 1))
                act.wait_ge(tr_ready, at(k))
                copy(yT[:, 0:n], M0[:, 0:n]).then_inc(y_done, 1)

            def slot(k, q, l1=True, l2=True, l3=True, n1=CH, n2=CH, n3=CH):
                for p in range(NPAIR):
                    if l1:
                        h1_high(k, q, p, n1)
                if l3:
                    y_copy(k - 2, n3)
                for p in range(NPAIR):
                    if l2:
                        r_act(k - 1, p, n2)
                        if p > 0:
                            t_high(k - 1, p - 1, n2)
                if l2:
                    t_high(k - 1, NPAIR - 1, n2)

            slot(0, 0, l2=False, l3=False)
            slot(1, 1, l3=False)
            slot(2, 0)
            slot(3, 1)
            with act.Fori(2, NB) as b:
                slot(2 * b, 0)
                slot(2 * b + 1, 1)
            slot(2 * NB, 0, n1=8)
            slot(2 * NB + 1, 1, l1=False, n2=8)
            y_copy(2 * NB, 8)

        @block.vector
        def _(dve):
            dve.wait_ge(ld_first, 48)
            dve.tensor_copy(identR[:, :], ident[:, :]).then_inc(dve_steps, 1)
            dve.wait_ge(ld_w, 64)
            dve.reduce_sum(st[:, 0, 0:1], c0B[:, :], AX).then_inc(dve_steps, 1)
            dve.wait_ge(dve_steps, nth("c_sum", 1))
            dve.tensor_scalar(st[:, 0, 0:1], st[:, 0, 0:1], -1.0 / D, None, ALU.mult).then_inc(dve_steps, 1)
            dve.wait_ge(dve_steps, nth("c_mean", 1))
            dve.tensor_scalar(c1B[:, :], c0B[:, :], st[:, 0, 0:1], None, ALU.add).then_inc(dve_steps, 1)
            dve.wait_ge(wt_copied, 2)
            for r in range(5):
                dve.wait_ge(evn_sum, at(r))
                dve.tensor_tensor(prE, WTe, bct(dft[:, r, 0:2 * EVEN], D), ALU.mult).then_inc(evn_mul, 1)
                dve.wait_ge(evn_mul, at(r + 1))
                dve.reduce_sum(sumE[:, r, :], prE, AX).then_inc(evn_sum, 1)
                dve.wait_ge(odd_mul, at(r + 1))
                dve.reduce_sum(sumO[:, r, :], prO, AX).then_inc(odd_sum, 1)
            dve.wait_ge(evn_sum, 5)
            dve.wait_ge(odd_sum, 5)
            dve.tensor_tensor(Wef[:, :, 0, :], sumE, sumO, ALU.add).then_inc(dve_steps, 1)
            dve.tensor_tensor(Wef[:, :, 1, :], sumE, sumO, ALU.subtract).then_inc(dve_steps, 1)
            dve.wait_ge(act_steps, nth("ah_done", 2))
            for i in range(2):
                dve.tensor_tensor(AlR[:, i, :], A32[:, :], AhR[:, i, :].bitcast(F32), ALU.subtract).then_inc(dve_steps, 1)
            dve.wait_ge(act_steps, nth("c_sq", 1))
            dve.reduce_sum(st[:, 1, 0:1], e0B[:, :], AX).then_inc(dve_steps, 1)
            dve.wait_ge(pool_steps, nth("c_rstd", 1))
            dve.tensor_scalar(e0B[:, :], c1B[:, :], st[:, 3, 0:1], None, ALU.mult).then_inc(dve_steps, 1)
            dve.wait_ge(act_steps, nth("c_vecc", 2))
            dve.wait_ge(dve_steps, nth("c_e0", 1))
            dve.tensor_tensor(c1B[:, :], e0B[:, :], ag[:, 1, :], ALU.mult).then_inc(dve_steps, 1)
            dve.wait_ge(dve_steps, nth("c_w00p", 1))
            dve.reduce_sum(w00[:, :], c1B[:, :], AX).then_inc(dve_steps, 1)

            def h_second(b, c):
                dve.wait_ge(ha_done, at(2 * b + c + 1))
                hb = Hb(b, QG * c, QG)
                dve.tensor_tensor(hb, (M0, M1)[c][:, :].rearrange("p (t s d) -> p t s d", s=2, d=D)[:, :, 1, :], hb,
                                  ALU.add).then_inc(h_done, 1)

            def ln1_centre(b):
                dve.wait_ge(h_done, at(2 * b + 2))
                dve.sem_inc(passed_dve)
                dve.reduce_sum(st[:, 0, :], Hb(b), AX).then_inc(n1_sum, 1)
                dve.wait_ge(n1_sum, at(b + 1))
                dve.tensor_scalar(st[:, 0, :], st[:, 0, :], -1.0 / D, None, ALU.mult).then_inc(n1_mean, 1)
                dve.wait_ge(n1_mean, at(b + 1))
                dve.tensor_tensor(xc[:, :, :], Hb(b), bc(st[:, 0, :], D), ALU.add).then_inc(n1_cent, 1)

            def ln1_ss(b):
                dve.wait_ge(n1_sq, at(b + 1))
                dve.reduce_sum(st[:, 1, :], e32[:, :, :], AX).then_inc(n1_ss, 1)

            def ln1_e(b):
                dve.wait_ge(n1_rstd, at(b + 1))
                dve.tensor_tensor(e32[:, :, :], xc[:, :, :], bc(st[:, 3, :], D), ALU.mult).then_inc(e_done, 1)

            def ln1_sr(b, q):
                dve.wait_ge(prod_done, at(b + 1))
                dve.reduce_sum(sr[q][:, :, :], prod[:, :, :, :], AX).then_inc(sr_done, 1)
                dve.wait_ge(sr_done, at(b + 1))
                dve.reduce_max(r0max[:, bass.ds(b, 1)], sr[q][:, :, 1], AX).then_inc(r0_done, 1)

            def gl(b, c):
                dve.wait_ge(gh_done, at(2 * b + c + 1))
                dve.tensor_tensor(Gl[:, CH * c:CH * c + CH], M0[:, :], Gh[:, CH * c:CH * c + CH].bitcast(F32),
                                  ALU.subtract).then_inc(gl_done, 1)

            def smax(b, q, t):
                dve.wait_ge(s_ready, at(8 * b + t + 1))
                dve.reduce_max(rmax[:, t:t + 1], Sp[t % 2][:, :], AX).then_inc(max_done, 1)
                dve.wait_ge(max_done, at(8 * b + t + 1))
                dve.tensor_scalar(negm[q][:, t:t + 1], rmax[:, t:t + 1], sr[q][:, t, 0:1], -SCALE,
                                  ALU.max, ALU.mult).then_inc(negm_done, 1)

            def mask(b, q, t):
                dve.wait_ge(tri_done, at(8 * b + t + 1))
                dve.wait_ge(pt_ready, at(NCH * b + (chunks(t)[0][0])))
                n = 128 * (t + 1)
                dve.scalar_tensor_tensor(out=EP[:, 2, 0:n], in0=Sp[t % 2][:, 0:n], scalar=0.0, in1=EP[:, t % 2, 0:n],
                                         op0=ALU.not_equal, op1=ALU.mult,
                                         accum_out=rsum[q][:, t:t + 1]).then_inc(p_done, 1)

            def ptl(b, t):
                for i, k0, n in chunks(t):
                    dve.wait_ge(pth_done, at(NCH * b + i + 1))
                    g, tq = t // QG, t % QG
                    sl = (slice(None), slice(k0, k0 + n), slice(128 * tq, 128 * tq + 128))
                    dve.tensor_tensor(PTl[g][sl], PTp[i % 2][:, 0:128 * n].rearrange("p (k q) -> p k q", q=128),
                                      PTh[g][sl].bitcast(F32), ALU.subtract).then_inc(ptl_done, 1)

            def class_arg(b, q, g):
                ts = slice(QG * g, QG * g + QG)
                dve.wait_ge(pv_done, at(2 * b + g))
                dve.scalar_tensor_tensor(out=pz[:, 0, :], in0=sr[q][:, ts, 0], scalar=SCALE, in1=negm[q][:, ts],
                                         op0=ALU.mult, op1=ALU.add).then_inc(p0_arg, 1)

            def p0_rest(b, q, g):
                ts = slice(QG * g, QG * g + QG)
                dve.wait_ge(p0_exp, at(2 * b + g + 1))
                dve.scalar_tensor_tensor(out=pz[:, 2, :], in0=sr[q][:, ts, 0], scalar=0.0, in1=pz[:, 1, :],
                                         op0=ALU.not_equal, op1=ALU.mult).then_inc(p0_done, 1)
                dve.wait_ge(p0_done, at(2 * b + g + 1))
                dve.wait_ge(p_done, at(8 * b + 4 * g + 4))
                dve.scalar_tensor_tensor(out=pz[:, 3, :], in0=rsum[q][:, ts], scalar=EPS_SUM, in1=pz[:, 2, :],
                                         op0=ALU.add, op1=ALU.add).then_inc(tot_done, 1)
                dve.wait_ge(tot_done, at(2 * b + g + 1))
                dve.reciprocal(pz[:, 3, :], pz[:, 3, :]).then_inc(rinv_done, 1)
                dve.wait_ge(rinv_done, at(2 * b + g + 1))
                dve.tensor_tensor(pz[:, 4, :], pz[:, 2, :], pz[:, 3, :], ALU.mult).then_inc(a0_done, 1)

            def o_norm(b, g):
                dve.wait_ge(o_ready, at(2 * b + g + 1))
                dve.wait_ge(h2_done, at(2 * b + g))
                dve.tensor_tensor(ot[:, :, :], M1[:, 0:QG * D].rearrange("p (t d) -> p t d", d=D), bc(pz[:, 3, :], D),
                                  ALU.mult).then_inc(ot_done, 1)

            def ln2_centre(b):
                dve.wait_ge(h2_done, at(2 * b + 2))
                dve.sem_inc(passed_dve)
                dve.reduce_sum(st2[:, 0, :], Hb(b), AX).then_inc(n2_sum, 1)
                dve.wait_ge(n2_sum, at(b + 1))
                dve.tensor_scalar(st2[:, 0, :], st2[:, 0, :], -1.0 / D, None, ALU.mult).then_inc(n2_mean, 1)
                dve.wait_ge(n2_mean, at(b + 1))
                dve.tensor_tensor(xc2[:, :, :], Hb(b), bc(st2[:, 0, :], D), ALU.add).then_inc(n2_cent, 1)

            def ln2_ss(b):
                dve.wait_ge(n2_sq, at(b + 1))
                dve.reduce_sum(st2[:, 1, :], e232[:, :, :], AX).then_inc(n2_ss, 1)

            def ln2_e(b):
                dve.wait_ge(n2_rstd, at(b + 1))
                dve.tensor_tensor(e232[:, :, :], xc2[:, :, :], bc(st2[:, 3, :], D), ALU.mult).then_inc(e2_done, 1)

            h_second(0, 0)
            h_second(0, 1)
            ln1_centre(0)
            ln1_ss(0)
            ln1_e(0)
            ln1_sr(0, 0)
            gl(0, 0)
            gl(0, 1)
            smax(0, 0, 0)

            def body(b, q, first=False, last=False):
                for t in range(NT):
                    if t < NT - 1:
                        smax(b, q, t + 1)
                    elif not last:
                        smax(b + 1, 1 - q, 0)
                    mask(b, q, t)
                    if t > 0:
                        ptl(b, t - 1)
                    elif not first:
                        ptl(b - 1, NT - 1)
                    if not first:
                        if t == 0:
                            class_arg(b - 1, 1 - q, 1)
                        if t == 1:
                            p0_rest(b - 1, 1 - q, 1)
                        if t == 2:
                            o_norm(b - 1, 1)
                        if t == 4:
                            ln2_centre(b - 1)
                        if t == 5:
                            ln2_ss(b - 1)
                        if t == 6:
                            ln2_e(b - 1)
                    if t == 4:
                        class_arg(b, q, 0)
                    if t == 5:
                        p0_rest(b, q, 0)
                    if t == 6:
                        o_norm(b, 0)
                    if not last:
                        if t == 3:
                            h_second(b + 1, 0)
                            h_second(b + 1, 1)
                            ln1_centre(b + 1)
                        if t == 4:
                            ln1_ss(b + 1)
                        if t == 5:
                            ln1_e(b + 1)
                        if t == 6:
                            ln1_sr(b + 1, 1 - q)
                            gl(b + 1, 0)
                            gl(b + 1, 1)

            body(0, 0, first=True)
            with dve.Fori(0, NB // 2 - 1) as j:
                body(2 * j + 1, 1)
                body(2 * j + 2, 0)
            body(NB - 1, 1, last=True)
            b = NB - 1
            ptl(b, NT - 1)
            class_arg(b, 1, 1)
            p0_rest(b, 1, 1)
            o_norm(b, 1)

            dve.wait_ge(pe_steps, nth("k_r0T", 1))
            dve.reduce_max(clsS[:, 0:1], PTp[0][0:8, 0:128], AX).then_inc(dve_steps, 1)
            dve.wait_ge(dve_steps, nth("k_max", 1))
            dve.tensor_scalar(clsS[:, 1:2], clsS[:, 0:1], w00[0:8, 0:1], -SCALE, ALU.max, ALU.mult).then_inc(dve_steps, 1)
            dve.wait_ge(dve_steps, nth("k_max2", 1))
            dve.scalar_tensor_tensor(out=clsS[:, 2:3], in0=w00[0:8, 0:1], scalar=SCALE, in1=clsS[:, 1:2],
                                     op0=ALU.mult, op1=ALU.add).then_inc(dve_steps, 1)
            dve.wait_ge(act_steps, nth("k_exp", 1))
            dve.scalar_tensor_tensor(out=clsS[:, 4:5], in0=w00[0:8, 0:1], scalar=0.0, in1=clsS[:, 3:4],
                                     op0=ALU.not_equal, op1=ALU.mult).then_inc(dve_steps, 1)
            dve.wait_ge(dve_steps, nth("k_p0", 1))
            dve.tensor_scalar(clsS[:, 5:6], clsS[:, 4:5], EPS_SUM, None, ALU.add).then_inc(dve_steps, 1)
            dve.wait_ge(dve_steps, nth("k_tot", 1))
            dve.reciprocal(clsS[:, 5:6], clsS[:, 5:6]).then_inc(dve_steps, 1)
            dve.wait_ge(dve_steps, nth("k_rc", 1))
            dve.tensor_tensor(clsS[:, 6:7], clsS[:, 4:5], clsS[:, 5:6], ALU.mult).then_inc(dve_steps, 1)

            ln2_centre(b)
            ln2_ss(b)
            ln2_e(b)

            dve.wait_ge(pool_steps, nth("k_h2", 1))
            dve.reduce_sum(clsS[:, 7:8], h2c[:, :], AX).then_inc(dve_steps, 1)
            dve.wait_ge(dve_steps, nth("k_sum", 1))
            dve.tensor_scalar(clsS[:, 8:9], clsS[:, 7:8], -1.0 / D, None, ALU.mult).then_inc(dve_steps, 1)
            dve.wait_ge(dve_steps, nth("k_mean", 1))
            dve.tensor_scalar(ccx[:, :], h2c[:, :], clsS[:, 8:9], None, ALU.add).then_inc(dve_steps, 1)
            dve.wait_ge(act_steps, nth("k_sq", 1))
            dve.reduce_sum(clsS[:, 9:10], e2c[:, :], AX).then_inc(dve_steps, 1)
            dve.wait_ge(pool_steps, nth("k_rstd", 1))
            dve.tensor_scalar(e2c[:, :], ccx[:, :], clsS[:, 11:12], None, ALU.mult).then_inc(dve_steps, 1)

            dve.wait_ge(pe_steps, nth("q_lg", 1))
            dve.tensor_tensor(gl9[:, :, :], Sp[1][:, 0:72].rearrange("p (t e) -> p t e", e=NEXP), bct(brB[:, :], 9),
                              ALU.add).then_inc(dve_steps, 1)
            dve.wait_ge(dve_steps, nth("q_lgb", 1))
            dve.reduce_max(gs9[:, 0, :], gl9[:, :, :], AX).then_inc(dve_steps, 1)
            dve.wait_ge(dve_steps, nth("q_mx", 1))
            dve.tensor_tensor(gl9[:, :, :], gl9[:, :, :], bc(gs9[:, 0, :], NEXP), ALU.subtract).then_inc(dve_steps, 1)
            dve.wait_ge(act_steps, nth("q_exp", 1))
            dve.reduce_sum(gs9[:, 1, :], gl9[:, :, :], AX).then_inc(dve_steps, 1)
            dve.wait_ge(dve_steps, nth("q_sum", 1))
            dve.reciprocal(gs9[:, 2, :], gs9[:, 1, :]).then_inc(dve_steps, 1)
            dve.wait_ge(dve_steps, nth("q_rc", 1))
            dve.tensor_tensor(gw9[:, :, :], gl9[:, :, :], bc(gs9[:, 2, :], NEXP), ALU.mult).then_inc(dve_steps, 1)
            dve.wait_ge(dve_steps, nth("q_w", 1))

            def spread(i):
                w_ = gw9[:, 0:NT, 2 * i:2 * i + 2].unsqueeze(3).to_broadcast([128, NT, 2, D])
                dve.tensor_copy(gx[i % 2].rearrange("p t (s d) -> p t s d", s=2), w_).then_inc(dve_steps, 1)

            spread(0)
            spread(1)
            dve.tensor_copy(gx8.rearrange("p a (s d) -> p (a s) d", s=2), bc(gw9[:, NT, :], D)).then_inc(dve_steps, 1)
            for i in (2, 3):
                dve.wait_ge(pe_steps, nth("q_bc", i - 1))
                spread(i)
            dve.wait_ge(pe_steps, nth("q_wb", 1))
            dve.tensor_copy(wob[:, 0:NT, :], M1[:, :].rearrange("p (t d) -> p t d", d=D))
            dve.tensor_copy(wob[:, NT, :], PTp[1][:, 128:128 + D]).then_inc(dve_steps, 1)

            def t2_copy(k, q, b, c):
                dve.wait_ge(l1_ready, at(4 * (k - 1)))
                dve.tensor_copy(T2[q][0:64, :], E2T[0:64, bass.ds(b, 1), CH * c:CH * c + CH].rearrange("p a n -> p (a n)").bitcast(F32))\
                    .then_inc(t2_done, 1)

            def h1_low(k, q, p, n=CH):
                dve.wait_ge(h1h_done, at(4 * k + p + 1))
                dve.scalar_tensor_tensor(out=h1l[q][:, p, 0:n], in0=L1p[p][:, 0:n], scalar=0.0,
                                         in1=h1h[q][:, p, 0:n].bitcast(F32), op0=ALU.max,
                                         op1=ALU.subtract).then_inc(h1l_done, 1)

            def gated(k, b, c, p, n=CH):
                dve.wait_ge(r_done, at(4 * k + p + 1))
                dve.wait_ge(tl_done, at(4 * k + p - 1))
                dve.tensor_tensor(t2[:, p % 2, 0:n], r2[:, p, 0:n], WB[:, p, CH * c:CH * c + n], ALU.mult).then_inc(t_done, 1)

            def out_add(k, b, c):
                dve.wait_ge(tr_ready, at(k + 1))
                dve.wait_ge(hw_done, at(k + 1))
                dve.wait_ge(st_half[c], at(16 * b))
                y = M1[:, :].rearrange("p (t s d) -> p t s d", s=2, d=D)
                dve.tensor_tensor(O32[c][:, :, :], y[:, :, 0, :], Hb(b, QG * c, QG), ALU.add).then_inc(oa_done, 1)
                dve.wait_ge(oa_done, at(k + 1))
                dve.tensor_tensor(O32[c][:, :, :], y[:, :, 1, :], O32[c][:, :, :], ALU.add).then_inc(o_done, 1)

            def slot(k, b, c, l1=True, l2=True, l3=True):
                if l1:
                    for p in range(NPAIR):
                        h1_low(k, c, p)
                if l3:
                    out_add(k - 3, b - 2 if c == 0 else b - 1, 1 - c)
                for p in range(NPAIR):
                    if l2:
                        gated(k - 1, b - 1 if c == 0 else b, 1 - c, p)

            dve.wait_ge(act_steps, nth("t2_set", 2))
            t2_copy(0, 0, 0, 0)
            t2_copy(1, 1, 0, 1)
            dve.wait_ge(act_steps, nth("q_bcc", 5))
            slot(0, 0, 0, l2=False, l3=False)
            t2_copy(2, 0, 1, 0)
            slot(1, 0, 1, l3=False)
            t2_copy(3, 1, 1, 1)
            slot(2, 1, 0, l3=False)
            t2_copy(4, 0, 2, 0)
            slot(3, 1, 1)
            t2_copy(5, 1, 2, 1)
            slot(4, 2, 0)
            t2_copy(6, 0, 3, 0)
            slot(5, 2, 1)
            t2_copy(7, 1, 3, 1)
            with dve.Fori(3, NB - 1) as b:
                slot(2 * b, b, 0)
                t2_copy(2 * b + 2, 0, b + 1, 0)
                slot(2 * b + 1, b, 1)
                t2_copy(2 * b + 3, 1, b + 1, 1)
            slot(2 * NB - 2, NB - 1, 0)
            dve.wait_ge(l1_ready, at(8 * NB - 4))
            dve.tensor_copy(T2[0][0:64, 0:8], e2cT[0:64, :].bitcast(F32)).then_inc(t2_done, 1)
            slot(2 * NB - 1, NB - 1, 1)
            for p in range(NPAIR):
                h1_low(2 * NB, 0, p, 8)
            out_add(2 * NB - 3, NB - 2, 1)
            for p in range(NPAIR):
                gated(2 * NB - 1, NB - 1, 1, p)
            out_add(2 * NB - 2, NB - 1, 0)
            for p in range(NPAIR):
                gated(2 * NB, None, 2, p, 8)
            out_add(2 * NB - 1, NB - 1, 1)
            dve.wait_ge(tr_ready, at(2 * NB + 1))
            dve.wait_ge(hw_done, at(2 * NB + 1))
            dve.tensor_tensor(Oc[:, :], M1[0:8, 0:D], h2c[:, :], ALU.add).then_inc(oa_done, 1)
            dve.wait_ge(oa_done, at(2 * NB + 1))
            dve.tensor_tensor(Oc[:, :], M1[0:8, D:2 * D], Oc[:, :], ALU.add).then_inc(o_done, 1)

        @block.tensor
        def _(pe):
            ON = dict(start=True, stop=True)

            pe.wait_ge(ld_first, 48)
            order = [NF * i + g for i in range(2) for g in range(0, NF, 2)] + [NF * i + g for i in range(2) for g in range(1, NF, 2)]
            for n, gidx in enumerate(order):
                bank, c0 = (Sp[0], D * n) if n < 5 else (Sp[0], CH + D * (n - 5)) if n < 10 else (Sp[1], D * (n - 10))
                for row in (0, 64):
                    ins = pe.matmul(bank[row:row + 64, c0:c0 + D], Wraw[:, gidx, :], ident[0:64, 0:64], **ON)
                if n in (4, 9, 17):
                    ins.then_inc(pe_steps, 1)
            pe.wait_ge(ld_w, 64)
            pe.wait_ge(ld_bn, 160)
            pe.transpose(M1[:, 320:360], bnr[:, :], ident[0:40, 0:40]).then_inc(pe_steps, 1)
            pe.matmul(M1[0:64, D:2 * D], qkv[:, 1, :], qkv[:, 0, :], **ON)
            for row in (0, 64):
                pe.matmul(M1[row:row + 64, 0:D], qkv[:, 0, :], qkv[:, 1, :], **ON)
                ins = pe.matmul(M1[row:row + 64, 2 * D:3 * D], qkv[:, 2, :], ident[0:64, 0:64], **ON)
            ins.then_inc(pe_steps, 1)
            def y_half(b, c, rs=range(4)):
                if 0 not in rs:
                    pass
                elif c == 0:
                    pe.wait_ge(ld_x, at(32 * b + 32))
                    pe.wait_ge(gl_done, at(2 * b))
                else:
                    pe.wait_ge(z_done, at(3 * b + 1))
                for r in rs:
                    ins = pe.matmul(M0[:, :], Wef[:, r, :, :], X[:, 8 * c:8 * c + 8, r, :], start=(r == 0), stop=(r == 3),
                                    skip_group_check=True)
                if 3 in rs:
                    ins.then_inc(y_ready, 1)

            def y_pad(b):
                pe.wait_ge(z_done, at(3 * b + 2))
                pe.matmul(M0[64:128, 0:V], Wef[:, 4, 1, :], X[:, 15, 3, :], **ON).then_inc(y_ready, 1)

            def z_turn(b, c):
                pe.wait_ge(z_done, at(3 * b + 3))
                if c == 1:
                    pe.wait_ge(ot_done, at(2 * (b - 1)))
                for i in range(QG):
                    t = QG * c + i
                    ins = pe.transpose((M0, M1)[c][:, 128 * i:128 * i + 128], Z[:, 128 * t:128 * t + 128], ident[:, :])
                ins.then_inc(zt_ready, 1)

            def e_turn(b, q, c):
                if c == 0:
                    pe.wait_ge(el_done, at(b + 1))
                    pe.wait_ge(h_done, at(2 * b + 2))
                else:
                    pe.wait_ge(et_done, at(2 * b + 1))
                for i in range(QG):
                    ins = pe.transpose(M0[:, 128 * i:128 * i + 128].bitcast(F32R), ehl[q][:, QG * c + i, :], identR[:, :])
                ins.then_inc(et_ready, 1)

            def g_half(b, q, c):
                pe.wait_ge(et_done, at(2 * b + 2))
                pe.wait_ge(gl_done, at(2 * b + c))
                mv = eT[q][:, CH * c:CH * c + CH]
                pe.matmul(M0[:, :], AhR[:, :, :], mv, start=True, stop=False)
                pe.matmul(M0[:, :], AlR[:, :, :], mv, start=False, stop=True).then_inc(g_ready, 1)

            def score_right(b, q, t):
                pe.wait_ge(gl_done, at(2 * b + 1 + t // QG))
                pe.wait_ge(max_done, at(8 * b + t - 1))
                for w_, first_ in ((Gh, True), (Gl, False)):
                    pe.matmul(Sp[t % 2][:, CH:S], w_[:, 128 * t:128 * t + 128], eT[q][:, CH:S],
                              start=first_, stop=not first_, skip_group_check=True)

            def score(b, q, t):
                pe.wait_ge(gl_done, at(2 * b + 1 + t // QG))
                pe.wait_ge(p_done, at(8 * b + t - 1))
                for w_, first_ in ((Gh, True), (Gl, False)):
                    for n in range(1 if 2 <= t <= 5 else 2):
                        ins = pe.matmul(Sp[t % 2][:, CH * n:CH * n + CH], w_[:, 128 * t:128 * t + 128],
                                        eT[q][:, CH * n:CH * n + CH], start=first_, stop=not first_,
                                        skip_group_check=True)
                ins.then_inc(s_ready, 1)

            def p_turn(b, t):
                for i, k0, n in chunks(t):
                    pe.wait_ge(p_done, at(8 * b + t + 1))
                    pe.wait_ge(ptl_done, at(NCH * b + i - 1))
                    for k in range(n):
                        ins = pe.transpose(PTp[i % 2][:, 128 * k:128 * k + 128],
                                           EP[:, 2, 128 * (k0 + k):128 * (k0 + k) + 128], ident[:, :])
                    ins.then_inc(pt_ready, 1)

            def u_group(b, q, g, m1_tokens=0):
                pe.wait_ge(ptl_done, at(NCH * b + (NCH if g else QG)))
                pe.wait_ge(ot_done, at(2 * b + g))
                if g == 0:
                    pe.wait_ge(h_done, m1_tokens)
                nk = QG * (g + 1)
                for k in range(nk):
                    q0 = 128 * max(0, k - QG * g)
                    for pt in (PTh, PTl):
                        ins = pe.matmul(M1[:, q0:CH], ehl[q][:, k, :], pt[g][:, k, q0:CH],
                                        start=(k == 0 and pt is PTh), stop=(k == nk - 1 and pt is PTl),
                                        skip_group_check=True)
                ins.then_inc(u_ready, 1)

            def o_group(b, g):
                pe.wait_ge(u_done, at(2 * b + g + 1))
                for i in range(QG):
                    ins = pe.matmul(M1[:, D * i:D * i + D], UT[:, 128 * i:128 * i + 128], WVT[:, :], **ON)
                ins.then_inc(o_ready, 1)

            def e2_turn(b, c):
                if c == 0:
                    pe.wait_ge(e2l_done, at(b + 1))
                else:
                    pe.wait_ge(e2t_done, at(2 * b + 1))
                for i in range(QG):
                    ins = pe.transpose(M1[:, 128 * i:128 * i + 128].bitcast(F32R), e2hl[:, QG * c + i, :], identR[:, :])
                ins.then_inc(e2t_ready, 1)

            pe.wait_ge(dve_steps, nth("wef_done", 2))
            y_half(0, 0)
            pe.wait_ge(dve_steps, nth("c_e0", 1))
            pe.wait_ge(act_steps, nth("bn_Tc", 1))
            pe.transpose(M1[0:64, 3 * D:3 * D + 128], e0B[:, :], ident[:, :]).then_inc(pe_steps, 1)
            pe.wait_ge(act_steps, nth("c_e0Tc", 1))
            pe.matmul(M1[:, 0:D], e0T[:, :], AT32[:, :], **ON)
            pe.matmul(M1[:, D:2 * D], e0T[:, :], A32[0:64, :], **ON)
            pe.matmul(M1[:, 2 * D:3 * D], e0T[:, :], WVT[0:64, :], **ON).then_inc(pe_steps, 1)
            y_half(0, 1)
            y_pad(0)
            z_turn(0, 0)
            z_turn(0, 1)
            for n, dg in enumerate((dgs, dgc)):
                pe.wait_ge(pool_steps, nth("bn_diag", n + 1))
                pe.matmul(PTp[n][:, :], onesf[:, :], dg, **ON).then_inc(pe_steps, 1)
            pe.wait_ge(dve_steps, nth("tabR", 1))
            e_turn(0, 0, 0)
            e_turn(0, 0, 1)
            pe.wait_ge(dve_steps, nth("al_done", 2))
            g_half(0, 0, 0)
            g_half(0, 0, 1)
            pe.wait_ge(act_steps, nth("c_vecc", 2))
            score(0, 0, 0)
            score(0, 0, 1)
            score_right(0, 0, 2)

            def body(b, q, first=False, last=False, y_next=True):
                for t in range(NT):
                    if t <= 2:
                        score_right(b, q, t + 3)
                    if t < NT - 2:
                        score(b, q, t + 2)
                    p_turn(b, t)
                    if t == 1 and not first:
                        o_group(b - 1, 1)
                    if t == 5:
                        o_group(b, 0)
                    if not last:
                        if t == 0:
                            if first:
                                y_half(b + 1, 0)
                            else:
                                y_half(b + 1, 1, range(0, 2))
                        if t == 1:
                            y_half(b + 1, 1, range(0 if first else 2, 4))
                        if t == 2:
                            y_pad(b + 1)
                            z_turn(b + 1, 0)
                            z_turn(b + 1, 1)
                        if t == 5:
                            e_turn(b + 1, 1 - q, 0)
                        if t == 6:
                            e_turn(b + 1, 1 - q, 1)
                            g_half(b + 1, 1 - q, 0)
                            g_half(b + 1, 1 - q, 1)
                        if t >= NT - 2:
                            score(b + 1, 1 - q, t - (NT - 2))
                        if t == NT - 1:
                            score_right(b + 1, 1 - q, 2)
                    if t == 0 and not first:
                        u_group(b - 1, 1 - q, 1)
                    if t == 4:
                        u_group(b, q, 0, 2 * NB if last else 2 * b + 4)
                    if t == 7 and not first:
                        e2_turn_after(b - 1, 0)
                        if not last and y_next:
                            y_half(b + 2, 0, range(0, 2))
                        e2_turn_after(b - 1, 1)
                        if not last and y_next:
                            y_half(b + 2, 0, range(2, 4))
                    if t == 7 and first:
                        y_half(b + 2, 0)

            def e2_turn_after(b, c):
                if c == 0:
                    pe.wait_ge(ot_done, at(2 * b + 3))
                e2_turn(b, c)

            body(0, 0, first=True)
            with pe.Fori(0, NB // 2 - 2) as j:
                body(2 * j + 1, 1)
                body(2 * j + 2, 0)
            body(NB - 3, 1)
            body(NB - 2, 0, y_next=False)
            body(NB - 1, 1, last=True)
            b = NB - 1
            pe.wait_ge(r0_done, at(NB))
            pe.wait_ge(ptl_done, at(NCH * b + NCH))
            u_group(b, 1, 1)
            pe.transpose(PTp[0][0:8, 0:128], r0max[:, :], ident[:, :]).then_inc(pe_steps, 1)
            o_group(b, 1)
            pe.wait_ge(ot_done, at(2 * NB))
            e2_turn(b, 0)
            e2_turn(b, 1)

            pe.wait_ge(feat_done, at(NB + 1))
            for c in range(2):
                for i in range(QG):
                    t = QG * c + i
                    ins = pe.transpose(Sp[0][0:64, 128 * t:128 * t + 128], feat[:, t, :], ident[:, :])
                ins.then_inc(pe_steps, 1)
            pe.wait_ge(pool_steps, nth("k_el", 1))
            pe.wait_ge(e2t_done, at(2 * NB))
            pe.transpose(M1[:, 0:8].bitcast(F32R), e2cR[:, :], identR[0:8, 0:8]).then_inc(pe_steps, 1)
            pe.matmul(Sp[1][0:64, CH:CH + 128], e2c[:, :], cst[0:8, 0:1].to_broadcast([8, 128]), **ON).then_inc(pe_steps, 1)
            pe.wait_ge(act_steps, nth("q_fc", 2))
            for t in range(NT):
                pe.matmul(Sp[1][:, NEXP * t:NEXP * t + NEXP], FT[:, 128 * t:128 * t + 128], Wr_s[:, :], **ON)
            pe.wait_ge(act_steps, nth("q_cmc", 1))
            pe.matmul(Sp[1][:, NEXP * NT:NEXP * NT + NEXP], f64[:, :], Wr_s[:, :], **ON).then_inc(pe_steps, 1)
            pe.wait_ge(dve_steps, nth("q_w", 1))
            pe.wait_ge(dve_steps, nth("k_max", 1))
            for c in range(3):
                if c == 2:
                    pe.wait_ge(act_steps, nth("q_wTc", 1))
                for i in range(QG if c < 2 else 1):
                    ins = pe.transpose(PTp[c % 2][0:8, 128 * i:128 * i + 128], gw9[:, QG * c + i, :], ident[:, :])
                ins.then_inc(pe_steps, 1)
            pe.wait_ge(act_steps, nth("k_eTc", 1))
            for i in range(NPAIR):
                pe.wait_ge(dve_steps, nth("q_gx", (1, 2, 4, 5)[i]))
                pe.wait_ge(act_steps, nth("q_bcc", i - 1))
                for t in range(NT):
                    ins = pe.transpose(Sp[i % 2][:, 128 * t:128 * t + 128], gx[i % 2][:, t, :], ident[:, :])
                ins.then_inc(pe_steps, 1)
            for i in range(NPAIR):
                ins = pe.transpose(M0[:, 128 * i:128 * i + 128], gx8[:, i, :], ident[:, :])
            ins.then_inc(pe_steps, 1)
            pe.wait_ge(act_steps, nth("q_wTc", 3))
            for t in range(NT + 1):
                dst = M1[:, D * t:D * t + D] if t < NT else PTp[1][:, 128:128 + D]
                ins = pe.matmul(dst, wT[:, 128 * t:128 * t + 128], bo_s[:, :], **ON)
            ins.then_inc(pe_steps, 1)
            pe.wait_ge(dve_steps, nth("q_wbc", 1))
            pe.wait_ge(act_steps, nth("q_bcc", 5))
            pe.wait_ge(pool_steps, nth("bn_w1l", 1))
            pe.wait_ge(pool_steps, nth("bn_bl", 1))
            pe.wait_ge(pool_steps, nth("bn_w2l", 1))
            pe.wait_ge(pool_steps, nth("bn_wol", 1))

            def layer1(k, q, mv, n=CH):
                pe.wait_ge(t2_done, at(k + 1))
                for p in range(NPAIR):
                    pe.wait_ge(h1l_done, at(4 * k + p - 3))
                    pe.matmul(L1p[p][:, 0:n], W1A[:, 128 * p:128 * p + 128], mv, start=True, stop=False)
                    pe.matmul(L1p[p][:, 0:n], W1B[:, 128 * p:128 * p + 128], T2[q][:, 0:n], start=False, stop=True)\
                        .then_inc(l1_ready, 1)

            def layer2(k, q, n=CH):
                for p in range(NPAIR):
                    pe.wait_ge(r_done, at(4 * k + p - 1))
                    pe.wait_ge(h1l_done, at(4 * k + p + 1))
                    o_ = L2p[p % 2][:, 0:n]
                    pe.matmul(o_, W2h[:, p, :], h1h[q][:, p, 0:n], start=True, stop=False)
                    pe.matmul(o_, W2h[:, p, :], h1l[q][:, p, 0:n], start=False, stop=False)
                    pe.matmul(o_, W2l[:, p, :], h1h[q][:, p, 0:n], start=False, stop=True).then_inc(l2_ready, 1)

            def layer3(k, n=CH):
                pe.wait_ge(y_done, at(k))
                for p in range(NPAIR):
                    pe.wait_ge(tl_done, at(4 * k + p + 1))
                    pe.matmul(M0[:, 0:n], WoR[:, p, :, :], th[:, p, 0:n], start=(p == 0), stop=False)
                    ins = pe.matmul(M0[:, 0:n], WoR[:, p, :, :], tl[:, p, 0:n], start=False, stop=(p == NPAIR - 1))
                ins.then_inc(l3_ready, 1)

            def turn_out(k):
                pe.wait_ge(y_done, at(k + 1))
                pe.wait_ge(o_done, at(k))
                for i in range(QG):
                    ins = pe.transpose(M1[:, 128 * i:128 * i + 128], yT[:, 128 * i:128 * i + 128], ident[:, :])
                ins.then_inc(tr_ready, 1)

            def mv(b, c):
                return E2T[:, bass.ds(b, 1), CH * c:CH * c + CH].rearrange("p a n -> p (a n)")

            layer1(0, 0, mv(0, 0))
            layer1(1, 1, mv(0, 1))
            layer2(0, 0)
            layer1(2, 0, mv(1, 0))
            layer3(0)
            layer2(1, 1)
            turn_out(0)
            layer1(3, 1, mv(1, 1))
            layer3(1)
            layer2(2, 0)
            turn_out(1)
            with pe.Fori(2, NB) as b:
                layer1(2 * b, 0, mv(b, 0))
                layer3(2 * b - 2)
                layer2(2 * b - 1, 1)
                turn_out(2 * b - 2)
                layer1(2 * b + 1, 1, mv(b, 1))
                layer3(2 * b - 1)
                layer2(2 * b, 0)
                turn_out(2 * b - 1)
            k = 2 * NB
            layer1(k, 0, e2cT[:, :], 8)
            layer3(k - 2)
            layer2(k - 1, 1)
            turn_out(k - 2)
            layer3(k - 1)
            layer2(k, 0, 8)
            turn_out(k - 1)
            layer3(k, 8)
            pe.wait_ge(y_done, at(k + 1))
            pe.wait_ge(o_done, at(k))
            pe.transpose(M1[0:8, 0:128], yT[:, 0:8], ident[:, :]).then_inc(tr_ready, 1)


_INS = ['x', 'cls_tok', 'L0_tok_W', 'L0_attn_WQ', 'L0_attn_WK', 'L0_attn_WV', 'L0_ffn_Wr', 'L0_ffn_br', 'L0_ffn_W1',
        'L0_ffn_b1', 'L0_ffn_g1', 'L0_ffn_be1', 'L0_ffn_m1', 'L0_ffn_v1', 'L0_ffn_W2', 'L0_ffn_b2', 'L0_ffn_g2',
        'L0_ffn_be2', 'L0_ffn_m2', 'L0_ffn_v2', 'L0_ffn_Wo', 'L0_ffn_bo']
_OUTS = [((NB, S + 1, D), 'float32')]


def kernel(**inputs):
    import numpy as _np
    import concourse.bacc as _bacc
    from concourse import mybir as _mybir
    from concourse.bass_utils import run_bass_kernel_spmd as _run

    nc = _bacc.Bacc("TRN2", target_bir_lowering=False, num_devices=1)
    arrays, args = {}, []
    for name in _INS:
        arrays[f"in_{name}_dram"] = _np.ascontiguousarray(inputs[name])
    arrays["in_ident_dram"] = _np.eye(128, dtype=_np.float32)
    arrays["in_dft_dram"] = dft_table()
    for name, a in arrays.items():
        args.append(nc.dram_tensor(name, a.shape, _mybir.dt.from_np(a.dtype), kind="ExternalInput").ap())
    for i, (shape, dtype) in enumerate(_OUTS):
        dt = _mybir.dt.from_np(_np.dtype(dtype))
        args.append(nc.dram_tensor(f"out_{i}_dram", shape, dt, kind="ExternalOutput").ap())
    tower(nc, *args)
    r = _run(nc, [arrays], core_ids=[0])
    got = tuple(r.results[0][f"out_{i}_dram"] for i in range(len(_OUTS)))
    return got[0]
```
